# Optimizing a Trainium2 kernel written in Bass

```python
import numpy as np
import jax
import jax.numpy as jnp

def _softmax(x, axis=-1):
    return jax.nn.softmax(x, axis=axis)

def _gelu(x):
    return jax.nn.gelu(x, approximate=True)

def _silu(x):
    return jax.nn.silu(x)

def _sigmoid(x):
    return jax.nn.sigmoid(x)

def _layernorm(x, axis=-1, eps=1e-05):
    m = jnp.mean(x, axis=axis, keepdims=True)
    v = jnp.var(x, axis=axis, keepdims=True)
    return (x - m) / jnp.sqrt(v + eps)

def _scatter_add(tgt, idx, src, axis=0):
    return tgt.at[idx].add(src)

def _segment_sum(src, seg, n):
    return jax.ops.segment_sum(src, seg, n)
kernel_name = 'mk_macaron_d1_jaxref_r4_074989'

def setup_inputs(seed: int=0):
    np.random.seed(seed)
    _w = jnp.asarray

    def _L0_attn_setup():
        import jax, jax.numpy as jnp
        import numpy as np
        B, S, D, H = (4, 512, 256, 16)
        DH = D // H
        key = jax.random.key(seed)
        ks = jax.random.split(key, 9)
        sc = 0.02
        return {'x': jax.random.normal(ks[0], (B, S, D), jnp.float32), 'WQ': jax.random.normal(ks[1], (D, D), jnp.float32) * sc, 'bQ': jax.random.normal(ks[2], (D,), jnp.float32) * sc, 'WK': jax.random.normal(ks[3], (D, D), jnp.float32) * sc, 'bK': jax.random.normal(ks[4], (D,), jnp.float32) * sc, 'WV': jax.random.normal(ks[5], (D, D), jnp.float32) * sc, 'bV': jax.random.normal(ks[6], (D,), jnp.float32) * sc, 'WO': jax.random.normal(ks[7], (DH, D), jnp.float32) * sc, 'bO': jax.random.normal(ks[8], (D,), jnp.float32) * sc}
    _L0_attn_in = _L0_attn_setup()

    def _L0_ffn_setup():
        import jax, jax.numpy as jnp
        import numpy as np
        N_EXPERTS = 16
        TOP_K = 4
        HIDDEN = 256
        INTER = 128
        B, S = (2, 256)
        key = jax.random.key(seed)
        k1, k2, k3, k4, k5 = jax.random.split(key, 5)
        return {'hidden_states': jax.random.normal(k1, (B, S, HIDDEN), dtype=jnp.float32), 'gate_w': jax.random.normal(k2, (N_EXPERTS, HIDDEN), dtype=jnp.float32) * 0.02, 'w1': jax.random.normal(k3, (N_EXPERTS, HIDDEN, INTER), dtype=jnp.float32) * 0.02, 'w3': jax.random.normal(k4, (N_EXPERTS, HIDDEN, INTER), dtype=jnp.float32) * 0.02, 'w2': jax.random.normal(k5, (N_EXPERTS, INTER, HIDDEN), dtype=jnp.float32) * 0.02}
    _L0_ffn_in = _L0_ffn_setup()
    _d = {'L0_attn_x': _L0_attn_in['x'], 'L0_attn_WQ': _L0_attn_in['WQ'], 'L0_attn_bQ': _L0_attn_in['bQ'], 'L0_attn_WK': _L0_attn_in['WK'], 'L0_attn_bK': _L0_attn_in['bK'], 'L0_attn_WV': _L0_attn_in['WV'], 'L0_attn_bV': _L0_attn_in['bV'], 'L0_attn_WO': _L0_attn_in['WO'], 'L0_attn_bO': _L0_attn_in['bO'], 'L0_ffn_gate_w': _L0_ffn_in['gate_w'], 'L0_ffn_w1': _L0_ffn_in['w1'], 'L0_ffn_w3': _L0_ffn_in['w3'], 'L0_ffn_w2': _L0_ffn_in['w2']}
    _x0 = _d['L0_attn_x']
    _d['L0_attn_x'] = jax.random.normal(jax.random.fold_in(jax.random.key(seed), 1), (4, 1024, 256), dtype=_x0.dtype)
    del _x0
    return _d

def reference(L0_attn_x, L0_attn_WQ, L0_attn_bQ, L0_attn_WK, L0_attn_bK, L0_attn_WV, L0_attn_bV, L0_attn_WO, L0_attn_bO, L0_ffn_gate_w, L0_ffn_w1, L0_ffn_w3, L0_ffn_w2):

    def _L0_attn_ref(x, WQ, bQ, WK, bK, WV, bV, WO, bO):
        import jax, jax.numpy as jnp
        import numpy as np
        B, S, D, H = (4, 512, 256, 16)
        DH = D // H
        b, s, d = x.shape
        h, dh = (H, DH)
        Q = (x @ WQ + bQ).reshape(b, s, h, dh).transpose(0, 2, 1, 3)
        K = (x @ WK + bK).reshape(b, s, h, dh).transpose(0, 2, 1, 3)
        V = (x @ WV + bV).reshape(b, s, h, dh).transpose(0, 2, 1, 3)
        scale = jnp.sqrt(jnp.float32(dh))
        scores = jnp.einsum('bhqd,bhkd->bhqk', Q, K) / scale
        causal = jnp.tril(jnp.ones((s, s), dtype=bool))
        scores = jnp.where(causal, scores, jnp.float32(-100000.0))
        A = jax.nn.softmax(scores, axis=-1)
        Z = jnp.einsum('bhqk,bhkd->bhqd', A, V)
        out = jnp.einsum('bhsd,de->bse', Z, WO) + jnp.float32(h) * bO
        return out

    def _L0_ffn_ref(hidden_states, gate_w, w1, w3, w2):
        import jax, jax.numpy as jnp
        import numpy as np
        N_EXPERTS = 16
        TOP_K = 4
        HIDDEN = 256
        INTER = 128
        B, S = (2, 256)
        'DeepseekV3 MoE adapter forward: router -> sparse scores -> expert GLU MLP -> combine.'
        b, s, h = hidden_states.shape
        x = hidden_states.reshape(-1, h)
        logits = jnp.einsum('th,eh->te', x, gate_w)
        probs = jax.nn.softmax(logits, axis=-1)
        topk_w, topk_idx = jax.lax.top_k(probs, TOP_K)
        topk_w = topk_w / jnp.sum(topk_w, axis=-1, keepdims=True)
        one_hot = (topk_idx[..., None] == jnp.arange(N_EXPERTS)).astype(topk_w.dtype)
        scores = jnp.einsum('tk,tke->te', topk_w, one_hot)
        g = jnp.einsum('th,ehi->tei', x, w1)
        u = jnp.einsum('th,ehi->tei', x, w3)
        act = jax.nn.silu(g) * u
        expert_out = jnp.einsum('tei,eih->teh', act, w2)
        out = jnp.einsum('teh,te->th', expert_out, scores)
        return out.reshape(b, s, h)
    x = L0_attn_x
    x = x + 0.5 * _L0_ffn_ref(_layernorm(x, axis=-1), L0_ffn_gate_w, L0_ffn_w1, L0_ffn_w3, L0_ffn_w2)
    x = x + _L0_attn_ref(_layernorm(x, axis=-1), L0_attn_WQ, L0_attn_bQ, L0_attn_WK, L0_attn_bK, L0_attn_WV, L0_attn_bV, L0_attn_WO, L0_attn_bO)
    x = x + 0.5 * _L0_ffn_ref(_layernorm(x, axis=-1), L0_ffn_gate_w, L0_ffn_w1, L0_ffn_w3, L0_ffn_w2)
    return x

_drawn_inputs = setup_inputs


def setup_inputs(seed=0):
    import zlib

    import numpy as np

    out = dict(_drawn_inputs(seed))
    spreads = {}
    factors = {'L0_attn_WQ': 8.0,
     'L0_attn_bQ': 8.0,
     'L0_attn_WK': 8.0,
     'L0_attn_bK': 8.0,
     'L0_attn_WV': 6.879,
     'L0_attn_bV': 8.0,
     'L0_attn_WO': 5.379,
     'L0_ffn_gate_w': 8.0,
     'L0_ffn_w1': 8.0,
     'L0_ffn_w3': 8.0,
     'L0_ffn_w2': 8.0}
    for name, (base, spread) in spreads.items():
        noise = np.random.default_rng([zlib.crc32(name.encode()), seed]).standard_normal(out[name].shape)
        drawn = base * np.exp(spread * noise) if base else spread * noise
        out[name] = jnp.asarray(drawn.astype(out[name].dtype))
    for name, factor in factors.items():
        out[name] = (out[name] * factor).astype(out[name].dtype)
    return out
```

```python
from contextlib import ExitStack

import concourse.bass as bass
from concourse import mybir

F32 = mybir.dt.float32
F32R = mybir.dt.float32r
BF16 = mybir.dt.bfloat16
ALU = mybir.AluOpType
ACT = mybir.ActivationFunctionType
AX = mybir.AxisListType

P = 128
B, S, D = 4, 1024, 256
TOKENS = B * S
TILES = TOKENS // P
KT = D // P
CHUNK_TILES = 4
CHUNK = CHUNK_TILES * P
CHUNKS = TOKENS // CHUNK
E, TOP_K, INTER = 16, 4, 128
EPAD = 32
WCOLS = 2 * KT * INTER + D
WGROUP = 2
H, DH = 16, 16
QUAD = 4
QUADS = H // QUAD
QT = S // P
HALF = 512
EPS = 1e-5
EULER = 2.718281828459045
NEG = -1.0e30
Q_PART = [0, 0, 1, 0, 2, 1]
K_PART = [0, 1, 0, 2, 0, 1]
SROWS = DH * len(Q_PART)
MROWS = 2


class Steps:

    def __init__(self, eng, sem):
        self.eng, self.sem, self.n, self.base = eng, sem, 0, 0

    def then(self, ins, alone=False):
        ins.then_inc(self.sem, 1)
        self.n += 1
        self.eng.wait_ge(self.sem, self.base + self.n)
        if alone:
            self.eng.sem_inc(self.sem, 1)
            self.n += 1


class Norm:

    def __init__(self, nc, ctx, name):
        def sb(n, shape, dt):
            return ctx.enter_context(nc.sbuf_tensor(f"{name}_{n}", shape, dt, side="right"))

        def sem(n):
            return ctx.enter_context(nc.semaphore(f"{name}_{n}"))

        self.stats = sb("stats", [P, CHUNK_TILES, 6], F32)
        self.mv = sb("mv", [P, CHUNK_TILES, 2], F32)
        self.veps = sb("veps", [P, CHUNK_TILES], F32)
        self.power = sb("power", [P, CHUNK_TILES], F32)
        self.root = sb("root", [P, CHUNK_TILES], F32)
        self.rstd = sb("rstd", [P, CHUNK_TILES], F32)
        self.fix = sb("fix", [P, CHUNK_TILES], F32)
        self.xn = sb("xn", [P, CHUNK_TILES, D], F32)
        self.xt = sb("xt", [P, KT, CHUNK], F32)
        self.xt_hi = sb("xt_hi", [P, 2, KT, CHUNK], F32R)
        self.xt_lo = sb("xt_lo", [P, 2, KT, CHUNK], F32R)
        self.turned = ctx.enter_context(nc.psum_tensor(f"{name}_turned", [P, 2, HALF], F32))
        self.veps_ready = sem("veps_ready")
        self.root_ready = sem("root_ready")
        self.xn_ready = sem("xn_ready")
        self.turned_ready = sem("turned_ready")
        self.xt_ready = sem("xt_ready")
        self.hi_ready = sem("hi_ready")
        self.lo_ready = sem("lo_ready")

    def vector_stats(self, dve, steps, x_res, c, tiles):
        for j in tiles:
            ins = dve.bn_stats(self.stats[:, j, :], x_res[:, bass.ds(c * CHUNK_TILES + j, 1), :])
        if CHUNK_TILES - 1 not in tiles:
            return
        steps.then(ins, alone=True)
        for j in range(CHUNK_TILES):
            ins = dve.bn_aggr(self.mv[:, j, :], self.stats[:, j, :])
        steps.then(ins)
        dve.tensor_scalar(self.veps[:, :], self.mv[:, :, 1], EPS, None, ALU.add).then_inc(self.veps_ready, 1)

    def pool_start(self, pool):
        pool.memset(self.power[:, :], -0.5).then_inc(self.root_ready, 1)
        pool.wait_ge(self.root_ready, 1)

    def pool_root(self, pool, k):
        pool.wait_ge(self.veps_ready, k + 1)
        pool.tensor_tensor(self.root[:, :], self.veps[:, :], self.power[:, :], ALU.pow).then_inc(self.root_ready, 1)

    def vector_rstd(self, dve, steps, k):
        dve.wait_ge(self.root_ready, k + 2)
        steps.then(dve.tensor_tensor(self.fix[:, :], self.root[:, :], self.root[:, :], ALU.mult))
        steps.then(dve.tensor_tensor(self.fix[:, :], self.fix[:, :], self.veps[:, :], ALU.mult))
        steps.then(dve.tensor_scalar(self.fix[:, :], self.fix[:, :], -0.5, 1.5, ALU.mult, ALU.add))
        steps.then(dve.tensor_tensor(self.rstd[:, :], self.root[:, :], self.fix[:, :], ALU.mult))
        dve.wait_ge(self.xt_ready, k * CHUNK_TILES + 2)

    def vector_apply(self, dve, x_res, c, tiles):
        for j in tiles:
            dve.tensor_scalar(self.xn[:, j, :].rearrange("p (a d) -> p a d", a=1),
                              x_res[:, bass.ds(c * CHUNK_TILES + j, 1), :],
                              self.mv[:, j, 0:1], self.rstd[:, j:j + 1],
                              ALU.subtract, ALU.mult).then_inc(self.xn_ready, 1)

    def tensor_turn(self, pe, ident, j, k):
        pe.wait_ge(self.xn_ready, k * CHUNK_TILES + j + 1)
        pe.wait_ge(self.xt_ready, k * CHUNK_TILES + j + 1)
        for h in range(KT):
            ins = pe.transpose(self.turned[:, j % 2, h * P:(h + 1) * P], self.xn[:, j, h * P:(h + 1) * P], ident[:, :])
        ins.then_inc(self.turned_ready, 1)

    def scalar_start(self, act):
        act.sem_inc(self.xt_ready, 2)

    def scalar_copy(self, act, j, k):
        act.wait_ge(self.turned_ready, k * CHUNK_TILES + j + 1)
        act.activation(self.xt[:, :, j * P:(j + 1) * P],
                       self.turned[:, j % 2, 0:KT * P].rearrange("p (h t) -> p h t", h=KT),
                       ACT.Copy).then_inc(self.xt_ready, 1)

    def scalar_hi(self, act, k, par):
        act.wait_ge(self.xt_ready, (k + 1) * CHUNK_TILES + 2)
        act.activation(self.xt_hi[:, bass.ds(par, 1), :, :], self.xt[:, :, :].rearrange("p (a h) t -> p a h t", a=1),
                       ACT.Copy).then_inc(self.hi_ready, 1)

    def vector_lo(self, dve, k, par):
        dve.wait_ge(self.hi_ready, k + 1)
        dve.tensor_tensor(self.xt_lo[:, bass.ds(par, 1), :, :], self.xt[:, :, :].rearrange("p (a h) t -> p a h t", a=1),
                          self.xt_hi[:, bass.ds(par, 1), :, :].bitcast(F32), ALU.subtract).then_inc(self.lo_ready, 1)


def three_passes(pe, out, a_hi, a_lo, b_hi, b_lo, first, last):
    pe.matmul(out, a_hi, b_hi, start=first, stop=False)
    pe.matmul(out, a_lo, b_hi, start=False, stop=False)
    return pe.matmul(out, a_hi, b_lo, start=False, stop=last)


def ffn(nc, name, norm, x_in, x_res, ident, gate_w, w1, w3, w2, out):
    with ExitStack() as ctx:
        def sb(n, shape, dt):
            return ctx.enter_context(nc.sbuf_tensor(f"{name}_{n}", shape, dt))

        def ps(n, shape):
            return ctx.enter_context(nc.psum_tensor(f"{name}_{n}", shape, F32))

        def sem(n):
            return ctx.enter_context(nc.semaphore(f"{name}_{n}"))

        w_stage = sb("w_stage", [P, 2, WGROUP, WCOLS], F32)
        w_hi = sb("w_hi", [P, E, WCOLS], F32R)
        w_lo = sb("w_lo", [P, E, WCOLS], F32R)
        gate_rows = sb("gate_rows", [E, D], F32)
        gate_t = sb("gate_t", [P, KT, EPAD], F32)
        silu = sb("silu", [P, 2, CHUNK], F32)
        act_f = sb("act_f", [P, 2, CHUNK], F32)
        act_hi = sb("act_hi", [P, 2, CHUNK], F32R)
        act_lo = sb("act_lo", [P, 2, CHUNK], F32R)
        logit_t = sb("logit_t", [P, P], F32)
        logit = sb("logit", [P, CHUNK_TILES, E], F32)
        top8 = sb("top8", [P, CHUNK_TILES, 8], F32)
        shifted = sb("shifted", [P, CHUNK_TILES, E], F32)
        euler = sb("euler", [P, CHUNK_TILES * E], F32)
        expo = sb("expo", [P, CHUNK_TILES, E], F32)
        above = sb("above", [P, CHUNK_TILES, E], F32)
        n_above = sb("n_above", [P, CHUNK_TILES], F32)
        equal = sb("equal", [P, CHUNK_TILES, E], F32)
        place = sb("place", [P, CHUNK_TILES, E], F32)
        ones = sb("ones", [P, E], F32)
        total = sb("total", [P, CHUNK_TILES], F32)
        score = sb("score", [P, 2, CHUNK_TILES, E], F32)

        g_ps = ps("g_ps", [P, 2, HALF])
        u_ps = ps("u_ps", [P, 2, HALF])
        o_ps = ps("o_ps", [P, 2, HALF])

        x_loaded = [sem(f"x_loaded{c}") for c in range(CHUNKS)] if x_in is not None else []
        gate_loaded = sem("gate_loaded")
        w_loaded = [sem(f"w_loaded{i}") for i in range(2)]
        w_hi_ready = sem("w_hi_ready")
        w_lo_ready = sem("w_lo_ready")
        w_rest_ready = sem("w_rest_ready")
        gate_turned = sem("gate_turned")
        gate_ready = sem("gate_ready")
        steps_sem = sem("steps")
        logit_turned = sem("logit_turned")
        logit_copied = sem("logit_copied")
        logit_ready = sem("logit_ready")
        logit_taken = sem("logit_taken")
        shift_ready = sem("shift_ready")
        expo_ready = sem("expo_ready")
        first_expo_ready = sem("first_expo_ready")
        g_ready = sem("g_ready")
        u_ready = sem("u_ready")
        g_free = sem("g_free")
        u_free = sem("u_free")
        act_hi_ready = sem("act_hi_ready")
        act_lo_ready = sem("act_lo_ready")
        o_ready = [sem(f"o_ready{i}") for i in range(2)]
        o_free = [sem(f"o_free{i}") for i in range(2)]
        stored = sem("stored")

        block = ctx.enter_context(nc.Block())

        w_dmas = 2 * WGROUP + 1

        @block.sync
        def _(sp):
            def load_weights(g):
                if 2 <= g < 4:
                    sp.wait_ge(w_lo_ready, g - 1)
                if g >= 4:
                    sp.wait_ge(w_rest_ready, g - 3)
                n = KT * INTER
                for i, w in enumerate((w1, w3)):
                    for e in range(WGROUP):
                        sp.dma_start(w_stage[:, g % 2, e, i * n:(i + 1) * n].rearrange("p (k i) -> p k i", k=KT),
                                     w[g * WGROUP + e].rearrange("(k p) i -> p k i", p=P)).then_inc(w_loaded[g % 2], 16)
                es = slice(g * WGROUP, (g + 1) * WGROUP)
                sp.dma_start(w_stage[:, g % 2, :, 2 * n:], w2[es].rearrange("e p d -> p e d")).then_inc(w_loaded[g % 2], 16)

            sp.dma_start(gate_rows[:, :], gate_w).then_inc(gate_loaded, 16)
            if x_in is not None:
                x_view = x_in.rearrange("b (c j p) d -> (b c) p j d", p=P, j=CHUNK_TILES)
                sp.dma_start(x_res[:, 0:CHUNK_TILES, :], x_view[0]).then_inc(x_loaded[0], 16)
            load_weights(0)
            load_weights(1)
            if x_in is not None:
                for c in range(1, CHUNKS):
                    sp.dma_start(x_res[:, c * CHUNK_TILES:(c + 1) * CHUNK_TILES, :], x_view[c]).then_inc(x_loaded[c], 16)
            for g in range(2, E // WGROUP):
                load_weights(g)
            if out is not None:
                out_view = out.rearrange("b (c j p) d -> (b c) p j d", p=P, j=CHUNK_TILES)
                for c in range(CHUNKS):
                    sp.wait_ge(o_free[0], E * (c + 1) + 1)
                    sp.wait_ge(o_free[1], E * (c + 1) + 1)
                    sp.dma_start(out_view[c], x_res[:, c * CHUNK_TILES:(c + 1) * CHUNK_TILES, :]).then_inc(stored, 16)
                sp.wait_ge(stored, 16 * CHUNKS)

        @block.gpsimd
        def _(pool):
            norm.pool_start(pool)
            pool.memset(euler[:, :], EULER).then_inc(expo_ready, 1)
            pool.wait_ge(expo_ready, 1)

            def exponentials(k):
                pool.wait_ge(shift_ready, k + 1)
                pool.tensor_tensor(expo[:, :, :].rearrange("p j e -> p (j e)"), euler[:, :],
                                   shifted[:, :, :].rearrange("p j e -> p (j e)"), ALU.pow).then_inc(expo_ready, 1)

            norm.pool_root(pool, 0)
            for g in range(2, E // WGROUP):
                pool.wait_ge(w_hi_ready, g + 1)
                gs = slice(g * WGROUP, (g + 1) * WGROUP)
                pool.tensor_tensor(w_lo[:, gs, :], w_stage[:, g % 2, :, :], w_hi[:, gs, :].bitcast(F32),
                                   ALU.subtract).then_inc(w_rest_ready, 1)
                if g == 2:
                    norm.pool_root(pool, 1)
            exponentials(1)
            with pool.Fori(2, CHUNKS) as k:
                norm.pool_root(pool, k)
                exponentials(k)
            if out is None:
                norm.pool_root(pool, CHUNKS)

        @block.scalar
        def _(act):
            norm.scalar_start(act)
            act.sem_inc(g_free, 2)

            def prepare(k, par, e, router=True):
                if 3 <= e < 3 + CHUNK_TILES:
                    norm.scalar_copy(act, e - 3, k)
                if e == 7:
                    norm.scalar_hi(act, k, par)
                if e == 9 and router:
                    act.wait_ge(logit_turned, k + 1)
                    act.activation(logit_t[:, :], norm.turned[:, 0, 0:P], ACT.Copy).then_inc(logit_copied, 1)

            def expert(n, par):
                act.wait_ge(g_ready, n + 1)
                act.wait_ge(u_free, n + 1)
                act.activation(silu[:, par, :], g_ps[:, par, :], ACT.Silu).then_inc(g_free, 1)
                act.wait_ge(u_free, n + 3)
                act.wait_ge(o_ready[1], n + 1)
                act.activation(act_hi[:, par, :], act_f[:, par, :], ACT.Copy).then_inc(act_hi_ready, 1)

            def cut_weights(g):
                act.wait_ge(w_loaded[g % 2], 16 * w_dmas * (g // 2 + 1))
                act.activation(w_hi[:, g * WGROUP:(g + 1) * WGROUP, :], w_stage[:, g % 2, :, :],
                               ACT.Copy).then_inc(w_hi_ready, 1)

            cut_weights(0)
            for e in range(E):
                prepare(0, 0, e)
            act.wait_ge(shift_ready, 1)
            act.activation(expo[:, :, :], shifted[:, :, :], ACT.Exp).then_inc(first_expo_ready, 1)
            cut_weights(1)

            def chunk(c, prep, first=False, router=True):
                for e in range(E):
                    expert(c * E + e, e % 2)
                    if first and e % WGROUP == 0 and e // WGROUP + 2 < E // WGROUP:
                        cut_weights(e // WGROUP + 2)
                    if prep:
                        prepare(c + 1, (c + 1) % 2, e, router)

            chunk(0, True, True)
            with act.Fori(1, CHUNKS - 1) as c:
                chunk(c, True)
            chunk(CHUNKS - 1, out is None, router=False)

        @block.vector
        def _(dve):
            steps = Steps(dve, steps_sem)
            dve.sem_inc(u_free, 2)
            dve.sem_inc(o_free[0], 1)
            dve.sem_inc(o_free[1], 1)
            dve.memset(ones[:, :], 1.0)
            steps.then(dve.memset(gate_t[:, :, :], 0.0))

            def router(k):
                dve.wait_ge(logit_ready, k + 1)
                ins = dve.tensor_copy(logit[:, :, :],
                                      norm.turned[:, 1, 0:P].rearrange("p (j e) -> p j e", e=EPAD)[:, :, 0:E])
                ins.then_inc(logit_taken, 1)
                dve.wait_ge(logit_taken, 2 * k + 1)
                dve.sem_inc(logit_taken, 1)
                for j in range(CHUNK_TILES):
                    ins = dve.max(top8[:, j, :], logit[:, j, :])
                steps.then(ins)
                dve.tensor_tensor(shifted[:, :, :], logit[:, :, :],
                                  top8[:, :, 0:1].broadcast_to([P, CHUNK_TILES, E]),
                                  ALU.subtract).then_inc(shift_ready, 1)

            def choose():
                least = top8[:, :, TOP_K - 1:TOP_K].broadcast_to([P, CHUNK_TILES, E])
                dve.tensor_tensor(above[:, :, :], logit[:, :, :], least, ALU.is_gt)
                steps.then(dve.tensor_tensor(equal[:, :, :], logit[:, :, :], least, ALU.is_equal))
                steps.then(dve.tensor_reduce(n_above[:, :], above[:, :, :], AX.X, ALU.add))
                for j in range(CHUNK_TILES):
                    ins = dve.tensor_tensor_scan(place[:, j, :], ones[:, :], equal[:, j, :], n_above[:, j:j + 1],
                                                 ALU.mult, ALU.add)
                steps.then(ins)
                steps.then(dve.scalar_tensor_tensor(equal[:, :, :], place[:, :, :], float(TOP_K), equal[:, :, :],
                                                    ALU.is_le, ALU.mult))
                steps.then(dve.tensor_tensor(above[:, :, :], above[:, :, :], equal[:, :, :], ALU.add))

            def weigh_experts(par):
                steps.then(dve.tensor_tensor(expo[:, :, :], expo[:, :, :], above[:, :, :], ALU.mult))
                steps.then(dve.tensor_reduce(total[:, :], expo[:, :, :], AX.X, ALU.add))
                steps.then(dve.reciprocal(total[:, :], total[:, :]))
                steps.then(dve.scalar_tensor_tensor(
                    score[:, bass.ds(par, 1), :, :].rearrange("p a j e -> p (a j) e"), expo[:, :, :], 0.5,
                    total[:, :].rearrange("p (j a) -> p j a", a=1).broadcast_to([P, CHUNK_TILES, E]),
                    ALU.mult, ALU.mult))

            def prepare(k, par, e, c=None):
                x_chunk = k if c is None else c
                if e < 2:
                    norm.vector_stats(dve, steps, x_res, x_chunk, (2 * e, 2 * e + 1))
                if e == 2:
                    norm.vector_rstd(dve, steps, k)
                if e in (2, 3):
                    norm.vector_apply(dve, x_res, x_chunk, (2 * e - 4, 2 * e - 3))
                if e == 8:
                    norm.vector_lo(dve, k, par)
                if c is not None:
                    return
                if e == 11:
                    router(k)
                if e == 12:
                    choose()
                if e == 15:
                    dve.wait_ge(expo_ready, k + 1)
                    weigh_experts(par)

            def add_half(n, c, par, e, half):
                dve.wait_ge(o_ready[half], n + 3)
                dve.wait_ge(o_free[half], n + 1)
                for j in (2 * half, 2 * half + 1):
                    xs = x_res[:, bass.ds(c * CHUNK_TILES + j, 1), :]
                    ins = dve.scalar_tensor_tensor(
                        xs, o_ps[:, half, (j % 2) * D:(j % 2 + 1) * D].rearrange("p (a d) -> p a d", a=1),
                        score[:, bass.ds(par, 1), j, e:e + 1].rearrange("p a b -> p (a b)"),
                        xs, ALU.mult, ALU.add)
                ins.then_inc(o_free[half], 1)

            def expert(n, par, before):
                dve.wait_ge(g_free, n + 3)
                dve.wait_ge(u_ready, n + 1)
                dve.tensor_tensor(act_f[:, par, :], u_ps[:, par, :], silu[:, par, :], ALU.mult).then_inc(u_free, 1)
                if before is not None:
                    add_half(*before, 0)
                dve.wait_ge(act_hi_ready, n + 1)
                dve.wait_ge(o_ready[1], n + 1)
                dve.tensor_tensor(act_lo[:, par, :], act_f[:, par, :], act_hi[:, par, :].bitcast(F32),
                                  ALU.subtract).then_inc(act_lo_ready, 1)
                if before is not None:
                    add_half(*before, 1)

            def cut_weights(g):
                dve.wait_ge(w_hi_ready, g + 1)
                gs = slice(g * WGROUP, (g + 1) * WGROUP)
                dve.tensor_tensor(w_lo[:, gs, :], w_stage[:, g % 2, :, :], w_hi[:, gs, :].bitcast(F32),
                                  ALU.subtract).then_inc(w_lo_ready, 1)

            if x_in is not None:
                dve.wait_ge(x_loaded[0], 16)
            for e in range(E - 1):
                if e == 2:
                    dve.wait_ge(gate_turned, 1)
                    dve.tensor_copy(gate_t[:, :, 0:E],
                                    norm.turned[:, 0, 0:KT * E].rearrange("p (h e) -> p h e", h=KT)).then_inc(gate_ready, 1)
                if e == 8:
                    cut_weights(0)
                prepare(0, 0, e)
            dve.wait_ge(first_expo_ready, 1)
            weigh_experts(0)
            cut_weights(1)

            def chunk(c, first, prep, after=None):
                at = steps.n
                for e in range(E):
                    n = c * E + e
                    if e:
                        before = (n - 1, c, c % 2, e - 1)
                    else:
                        before = None if first else (n - 1, c - 1, (c + 1) % 2, E - 1)
                    expert(n, e % 2, before)
                    if first and e == 0 and x_in is not None:
                        for i in range(1, CHUNKS):
                            dve.wait_ge(x_loaded[i], 16)
                    if prep:
                        prepare(c + 1, (c + 1) % 2, e, after)
                return steps.n - at

            per = chunk(0, True, True)
            with dve.Fori(1, CHUNKS - 1) as c:
                at = steps.n
                steps.base = (c - 1) * per
                chunk(c, False, True)
                assert steps.n - at == per
            chunk(CHUNKS - 1, False, out is None, 0)
            n = CHUNKS * E
            for half in range(2):
                add_half(n - 1, CHUNKS - 1, (CHUNKS - 1) % 2, E - 1, half)

        @block.tensor
        def _(pe):
            pe.sem_inc(o_ready[0], 2)
            pe.sem_inc(o_ready[1], 2)
            pe.wait_ge(gate_loaded, 16)
            for h in range(KT):
                ins = pe.transpose(norm.turned[:, 0, h * E:(h + 1) * E], gate_rows[:, h * P:(h + 1) * P], ident[0:E, 0:E])
            ins.then_inc(gate_turned, 1)
            pe.wait_ge(gate_ready, 1)

            def prepare(k, e, router=True):
                if 3 <= e < 3 + CHUNK_TILES:
                    norm.tensor_turn(pe, ident, e - 3, k)
                if e == 8 and router:
                    pe.wait_ge(norm.xt_ready, (k + 1) * CHUNK_TILES + 2)
                    for h in range(KT):
                        for j in range(CHUNK_TILES):
                            ins = pe.matmul(norm.turned[j * EPAD:(j + 1) * EPAD, 0, 0:P], gate_t[:, h, :],
                                            norm.xt[:, h, j * P:(j + 1) * P], start=(h == 0), stop=(h == KT - 1))
                    ins.then_inc(logit_turned, 1)
                if e == 10 and router:
                    pe.wait_ge(logit_copied, k + 1)
                    pe.transpose(norm.turned[:, 1, 0:P], logit_t[:, :], ident[:, :]).then_inc(logit_ready, 1)

            def up(n, par, xpar, e, c):
                pe.wait_ge(w_hi_ready, e // WGROUP + 1)
                if e // WGROUP < 2:
                    pe.wait_ge(w_lo_ready, e // WGROUP + 1)
                else:
                    pe.wait_ge(w_rest_ready, e // WGROUP - 1)
                pe.wait_ge(norm.hi_ready, c + 1)
                pe.wait_ge(norm.lo_ready, c + 1)
                for i, (dst, free, ready) in enumerate(((g_ps, g_free, g_ready), (u_ps, u_free, u_ready))):
                    pe.wait_ge(free, n + 1)
                    for h in range(KT):
                        ws = slice((i * KT + h) * INTER, (i * KT + h + 1) * INTER)
                        xs = [t[:, bass.ds(xpar, 1), h, :].rearrange("p a t -> p (a t)") for t in (norm.xt_hi, norm.xt_lo)]
                        ins = three_passes(pe, dst[:, par, :], w_hi[:, e, ws], w_lo[:, e, ws],
                                           xs[0], xs[1], h == 0, h == KT - 1)
                    ins.then_inc(ready, 1)

            def down(n, par, e):
                pe.wait_ge(act_hi_ready, n + 1)
                pe.wait_ge(act_lo_ready, n + 1)
                for half in range(2):
                    pe.wait_ge(o_free[half], n + 1)
                    for j in (2 * half, 2 * half + 1):
                        ts = slice(j * P, (j + 1) * P)
                        ins = three_passes(pe, o_ps[:, half, (j % 2) * D:(j % 2 + 1) * D],
                                           act_hi[:, par, ts], act_lo[:, par, ts],
                                           w_hi[:, e, 2 * KT * INTER:], w_lo[:, e, 2 * KT * INTER:], True, True)
                    ins.then_inc(o_ready[half], 1)

            for e in range(E):
                prepare(0, e)

            def chunk(c, first, prep, router=True):
                for e in range(E):
                    n = c * E + e
                    up(n, e % 2, c % 2, e, c)
                    if e or not first:
                        down(n - 1, (e + 1) % 2, (e + E - 1) % E)
                    if prep:
                        prepare(c + 1, e, router)

            chunk(0, True, True)
            with pe.Fori(1, CHUNKS - 1) as c:
                chunk(c, False, True)
            chunk(CHUNKS - 1, False, out is None, False)
            down(CHUNKS * E - 1, (E - 1) % 2, E - 1)


class Rows:

    def __init__(self, nc, ctx, parts):
        self.nc, self.parts = nc, parts
        self.q = [ctx.enter_context(nc.sbuf_tensor(f"q_rows{q}", [P, QUAD, S], BF16)) for q in range(QUADS)]
        self.k = [ctx.enter_context(nc.sbuf_tensor(f"k_rows{q}", [P, QUAD, S], BF16)) for q in range(QUADS)]
        self.loaded = [ctx.enter_context(nc.semaphore(f"qk_loaded{q}")) for q in range(QUADS)]
        self.load_dmas = len(K_PART) + len(Q_PART)
        self.load_incs = 16 * self.load_dmas

    def load(self, sp, b, q, which):
        for g in which:
            rows, i, order = (self.k, 1, K_PART) if g < len(K_PART) else (self.q, 0, Q_PART)
            g %= len(K_PART)
            src = self.parts[i, order[g], q * QUAD * DH:(q + 1) * QUAD * DH, bass.ds(b * S, S)]
            sp.dma_start(rows[q][g * DH:(g + 1) * DH, :, :],
                         src.rearrange("(h d) t -> d h t", d=DH)).then_inc(self.loaded[q], 16)


def project(nc, norm, x_res, v_res, ident, weights, biases, parts, rows):
    with ExitStack() as ctx:
        def sb(n, shape, dt):
            return ctx.enter_context(nc.sbuf_tensor(f"proj_{n}", shape, dt))

        def sem(n):
            return ctx.enter_context(nc.semaphore(f"proj_{n}"))

        w_stage = sb("w_stage", [P, 3, KT, D], F32)
        w_hi = sb("w_hi", [P, 3, KT, D], F32R)
        w_lo = sb("w_lo", [P, 3, KT, D], F32R)
        bias_cols = sb("bias_cols", [P, 2, KT], F32)
        bias_v = sb("bias_v", [P, 2, D], F32)
        rest = sb("rest", [P, 4, CHUNK], F32)
        cut = sb("cut", [P, 4, 3, CHUNK], BF16)
        qk_ps = ctx.enter_context(nc.psum_tensor("proj_qk_ps", [P, 4, HALF], F32))
        v_ps = ctx.enter_context(nc.psum_tensor("proj_v_ps", [P, 2, HALF], F32))

        w_loaded = [sem(f"w_loaded{i}") for i in range(3)]
        biases_loaded = sem("biases_loaded")
        w_hi_ready = sem("w_hi_ready")
        w_lo_ready = sem("w_lo_ready")
        steps_sem = sem("steps")
        qk_ready = sem("qk_ready")
        first_ready = sem("first_ready")
        rest_ready = sem("rest_ready")
        second_ready = sem("second_ready")
        third_ready = sem("third_ready")
        stored = [sem(f"stored{i}") for i in range(4)]
        v_ready = sem("v_ready")
        v_free = sem("v_free")
        bias_loads = 2 + 2
        block = ctx.enter_context(nc.Block())

        @block.sync
        def _(sp):
            for i, w in enumerate(weights):
                sp.dma_start(w_stage[:, i, :, :], w.rearrange("(k p) n -> p k n", p=P)).then_inc(w_loaded[i], 16)
            with nc.allow_non_contiguous_dma(reason="two columns of biases"):
                for i in range(2):
                    sp.dma_start(bias_cols[:, i, :], biases[i].rearrange("(k p) -> p k", p=P)).then_inc(biases_loaded, 16)
            for i in range(2):
                sp.dma_start(bias_v[:, i, :], biases[2].rearrange("(a d) -> a d", a=1).broadcast_to([P, D])).then_inc(biases_loaded, 16)

            def store(c, load=None):
                for i in range(4):
                    if load is not None and i:
                        rows.load(sp, 0, load, range(4 * i - 4, 4 * i))
                    sp.wait_ge(third_ready, c * 4 + i + 5)
                    sp.dma_start(parts[i // 2, :, (i % 2) * P:(i % 2 + 1) * P, bass.ds(c * CHUNK, CHUNK)]
                                 .rearrange("r p t -> p r t"), cut[:, i, :, :]).then_inc(stored[i], 16)

            first = S // CHUNK
            for c in range(first):
                store(c)
            for done in stored:
                sp.wait_ge(done, 16 * (first + 1))
            for c in range(first, first + QUADS):
                store(c, c - first)
            with sp.Fori(first + QUADS, CHUNKS) as c:
                store(c)
            for done in stored:
                sp.wait_ge(done, 16 * (CHUNKS + 1))

        @block.scalar
        def _(act):
            for done in stored:
                act.sem_inc(done, 16)

            def second(c, i):
                act.wait_ge(rest_ready, c * 4 + i + 5)
                act.activation(cut[:, i, 1, :], rest[:, i, :], ACT.Copy).then_inc(second_ready, 1)

            def take(c, par, more):
                for i in range(4):
                    n = c * 4 + i
                    act.wait_ge(qk_ready, n + 1)
                    act.wait_ge(stored[i], 16 * (c + 1))
                    act.activation(cut[:, i, 0, :], qk_ps[:, i, :], ACT.Identity,
                                   bias=bias_cols[:, i // 2, i % 2:i % 2 + 1]).then_inc(first_ready, 1)
                    if more and i < 2:
                        norm.scalar_copy(act, 2 * i, CHUNKS + c + 1)
                        norm.scalar_copy(act, 2 * i + 1, CHUNKS + c + 1)
                    if more and i == 1:
                        norm.scalar_hi(act, CHUNKS + c + 1, par)
                    if i:
                        second(c, i - 1)
                second(c, 3)

            for i in range(3):
                act.wait_ge(w_loaded[i], 16)
                act.activation(w_hi[:, i, :, :], w_stage[:, i, :, :], ACT.Copy).then_inc(w_hi_ready, 1)
            act.wait_ge(biases_loaded, 16 * bias_loads)
            with act.Fori(0, CHUNKS - 1) as c:
                take(c, (c + 1) % 2, True)
            take(CHUNKS - 1, None, False)

        @block.gpsimd
        def _(pool):
            norm.pool_root(pool, CHUNKS + 1)
            pool.sem_inc(third_ready, 4)

            def third(c, i):
                pool.wait_ge(second_ready, c * 4 + i + 1)
                pool.tensor_tensor(cut[:, i, 2, :], rest[:, i, :], cut[:, i, 1, :],
                                   ALU.subtract).then_inc(third_ready, 1)

            with pool.Fori(0, CHUNKS - 2) as c:
                norm.pool_root(pool, CHUNKS + c + 2)
                for i in range(4):
                    third(c, i)
            for c in (CHUNKS - 2, CHUNKS - 1):
                for i in range(4):
                    third(c, i)

        @block.vector
        def _(dve):
            steps = Steps(dve, steps_sem)
            dve.sem_inc(v_free, 2)
            dve.memset(v_res[:, :, :, DH:DH + 1], 1.0)

            def stats(k):
                norm.vector_stats(dve, steps, x_res, k, range(CHUNK_TILES))

            def apply(k):
                norm.vector_rstd(dve, steps, CHUNKS + k)
                norm.vector_apply(dve, x_res, k, range(CHUNK_TILES))

            def rest_of(c, i):
                dve.wait_ge(first_ready, c * 4 + i + 1)
                dve.wait_ge(third_ready, c * 4 + i + 1)
                dve.scalar_tensor_tensor(rest[:, i, :], qk_ps[:, i, :], bias_cols[:, i // 2, i % 2:i % 2 + 1],
                                         cut[:, i, 0, :], ALU.add, ALU.subtract).then_inc(rest_ready, 1)

            def take_values(c, v):
                dve.wait_ge(v_ready, c * 2 + v + 1)
                dve.tensor_tensor(v_res[:, bass.ds(c * CHUNK_TILES + 2 * v, 2), :, 0:DH],
                                  v_ps[:, v, :].rearrange("p (j h d) -> p j h d", j=2, h=H),
                                  bias_v[:, :, :].rearrange("p j (h d) -> p j h d", h=H),
                                  ALU.add).then_inc(v_free, 1)

            dve.sem_inc(rest_ready, 4)
            stats(1)
            for i in range(3):
                dve.wait_ge(w_hi_ready, i + 1)
                dve.tensor_tensor(w_lo[:, i, :, :], w_stage[:, i, :, :], w_hi[:, i, :, :].bitcast(F32),
                                  ALU.subtract).then_inc(w_lo_ready, 1)
            apply(1)
            per = steps.n

            def chunk(c, par, split, norms):
                rest_of(c, 0)
                if norms:
                    stats(c + 2)
                rest_of(c, 1)
                if split:
                    norm.vector_lo(dve, CHUNKS + c + 1, par)
                rest_of(c, 2)
                if norms:
                    apply(c + 2)
                rest_of(c, 3)
                take_values(c, 0)
                take_values(c, 1)

            with dve.Fori(0, CHUNKS - 2) as c:
                steps.base = c * per
                chunk(c, (c + 1) % 2, True, True)
                assert steps.n == 2 * per
            chunk(CHUNKS - 2, (CHUNKS - 1) % 2, True, False)
            chunk(CHUNKS - 1, None, False, False)

        @block.tensor
        def _(pe):
            def project_chunk(c, more):
                pe.wait_ge(norm.hi_ready, CHUNKS + c + 1)
                pe.wait_ge(norm.lo_ready, CHUNKS + c + 1)
                xt = [[t[:, bass.ds(c % 2, 1), h, :].rearrange("p a t -> p (a t)") for t in (norm.xt_hi, norm.xt_lo)]
                      for h in range(KT)]
                for i in range(4):
                    pe.wait_ge(w_hi_ready, i // 2 + 1)
                    pe.wait_ge(w_lo_ready, i // 2 + 1)
                    pe.wait_ge(rest_ready, c * 4 + i + 1)
                    for h in range(KT):
                        ws = slice((i % 2) * P, (i % 2 + 1) * P)
                        ins = three_passes(pe, qk_ps[:, i, :], w_hi[:, i // 2, h, ws], w_lo[:, i // 2, h, ws],
                                           xt[h][0], xt[h][1], h == 0, h == KT - 1)
                    ins.then_inc(qk_ready, 1)
                    if more and i < 2:
                        norm.tensor_turn(pe, ident, 2 * i, CHUNKS + c + 1)
                        norm.tensor_turn(pe, ident, 2 * i + 1, CHUNKS + c + 1)

            def values(c, par):
                pe.wait_ge(w_hi_ready, 3)
                pe.wait_ge(w_lo_ready, 3)
                for v in range(2):
                    pe.wait_ge(v_free, c * 2 + v + 1)
                    for j in (2 * v, 2 * v + 1):
                        ts = slice(j * P, (j + 1) * P)
                        for h in range(KT):
                            ins = three_passes(pe, v_ps[:, v, (j % 2) * D:(j % 2 + 1) * D],
                                               norm.xt_hi[:, par, h, ts], norm.xt_lo[:, par, h, ts],
                                               w_hi[:, 2, h, :], w_lo[:, 2, h, :], h == 0, h == KT - 1)
                    ins.then_inc(v_ready, 1)

            with pe.Fori(0, CHUNKS // 2 - 1) as pair:
                for par in range(2):
                    project_chunk(pair * 2 + par, True)
                    values(pair * 2 + par, par)
            for c in (CHUNKS - 2, CHUNKS - 1):
                project_chunk(c, c < CHUNKS - 1)
                values(c, c % 2)


def attention(nc, x_res, v_res, ident, ident_b, mask_qk, wo, bo, rows):
    with ExitStack() as ctx:
        def sb(n, shape, dt):
            return ctx.enter_context(nc.sbuf_tensor(f"attn_{n}", shape, dt))

        def ps(n, shape):
            return ctx.enter_context(nc.psum_tensor(f"attn_{n}", shape, F32))

        def sem(n):
            return ctx.enter_context(nc.semaphore(f"attn_{n}"))

        q_rows, k_rows, qk_loaded = rows.q, rows.k, rows.loaded
        v_now = sb("v_now", [P, QUADS, QT, QUAD * (DH + 1)], F32)
        PROB = [0, 1, 2, 0, 1, 2, 3, 4]
        prob = [sb(f"prob{i}", [P, QUAD, S - PROB.index(i) * P], F32) for i in range(max(PROB) + 1)]
        max_a = sb("max_a", [P, 2, QUAD, QT], F32)
        max_b = sb("max_b", [P, 2, QUAD, QT // 2], F32)
        neg_max = sb("neg_max", [QUAD * QT, P], F32)
        max_parts = sb("max_parts", [QUAD * QT, MROWS, P], BF16)
        o_sb = sb("o_sb", [P, S], F32)
        values = sb("values", [P, QT, QUAD, DH + 1], F32)
        inv = sb("inv", [P, QT, QUAD, 1], F32)
        weighted = sb("weighted", [P, QT, QUAD, DH], F32)
        pairs = sb("pairs", [P, QT, 2, DH], F32)
        z = sb("z", [P, QT, 32], F32)
        z_t = sb("z_t", [P, 2, P], F32)
        wo_block = sb("wo_block", [P, QT // 2, D], F32)

        a_ps = ps("a_ps", [P, 2, HALF])
        b_ps = ps("b_ps", [P, 2, S])
        o_ps = ps("o_ps", [P, S])

        wo_zeroed = sem("wo_zeroed")
        wo_loaded = sem("wo_loaded")
        ones_ready = sem("ones_ready")
        o_zeroed = sem("o_zeroed")
        a_ready = sem("a_ready")
        a_free = sem("a_free")
        b_ready = sem("b_ready")
        b_free = sem("b_free")
        masked = sem("masked")
        mask_begun = sem("mask_begun")
        v_copied = sem("v_copied")
        pv_ready = sem("pv_ready")
        o_copied = sem("o_copied")
        inv_ready = sem("inv_ready")
        values_taken = sem("values_taken")
        max_ready = sem("max_ready")
        max_cut = sem("max_cut")
        max_loaded = sem("max_loaded")
        z_ready = sem("z_ready")
        z_turned = sem("z_turned")
        steps_sem = sem("steps")
        pool_steps_sem = sem("pool_steps")
        block = ctx.enter_context(nc.Block())

        slots = []
        for kt in range(QT):
            heads = 1 if kt < 4 else 2 if kt < 6 else 4
            slots += [(kt, h, heads) for h in range(0, QUAD, heads)]
        steps_n = len(slots)
        last_slot = [max(n for n, slot in enumerate(slots) if slot[0] == kt) for kt in range(QT)]
        banks = []
        for qt in reversed(range(QT)):
            keys = (qt + 1) * P
            for first in range(0, keys, HALF):
                width = min(HALF, keys - first)
                heads = HALF // width
                banks += [(qt, first, width, first + width == keys, h, heads) for h in range(0, QUAD, heads)]
        beside_n = [2, 1, 2, 2, 2, 2, 1, 2, 1, 2, 2, 1, 2, 2, 1, 2, 2, 1, 2, 2, 2, 2]
        AHEAD = 16
        assert sum(beside_n) == len(banks)
        early = sum(beside_n[AHEAD:])

        def beside(n):
            at = sum(beside_n[AHEAD:n]) if n >= AHEAD else early + sum(beside_n[:n])
            return banks[at:at + beside_n[n]], 2 if n >= AHEAD else 1

        QUARTER = HALF // 2

        def quarters(kt):
            qs = list(range(kt * P // QUARTER, S // QUARTER))
            return qs[1:] + qs[:1]

        WEIGH = [(6, 7, 8, 9), (10, 11, 12, 13), (14, 15, 16), (17, 18, 19), (20, 21), (22, 23), (24,), (25,)]
        LEAD = 12
        COPY_AT, TURN_AT, INVERT_AT, OUTPUT_AT = 3, 5, 6, 10
        lead_kts = sum(last < LEAD for last in last_slot)
        a_first = len(banks) + early + 1 + sum(beside_n[:LEAD])
        a_seq = QUADS * (len(banks) + 1) + 2 + QT // 2
        assert a_seq % 2 == 0
        b_unit = steps_n + 1
        assert b_unit * QUADS % 2 == 0

        def prob_at(kt, query):
            return query - PROB.index(PROB[kt]) * P

        class Ring:

            def __init__(self):
                self.base, self.n, self.odd = 0, 0, 0

            def take(self):
                bank, number = (self.odd + self.n) % 2, self.base + self.n
                self.n += 1
                return bank, number

            def sequence(self, b):
                self.base, self.n, self.odd = a_first + b * a_seq, 0, a_first % 2

        def b_place(b, q, n, first=False):
            at = q * b_unit + n - 1 + (n > TURN_AT) + (first and n <= TURN_AT)
            return at % 2, b * QUADS * b_unit + at

        def b_place_values(b, q, more):
            at = (q + 1) * b_unit + (TURN_AT if more else -1)
            return at % 2, b * QUADS * b_unit + at

        @block.sync
        def _(sp):
            def load_max(u, q):
                sp.wait_ge(max_cut, u + 1)
                for r in range(MROWS):
                    sp.dma_start(q_rows[q][SROWS + r:SROWS + r + 1, :, :].rearrange("p h (t c) -> p (h t) c", c=P),
                                 max_parts[:, r, :]).then_inc(max_loaded, 16)

            sp.wait_ge(wo_zeroed, 1)
            sp.wait_ge(o_zeroed, 1)
            for j in range(QT // 2):
                sp.dma_start(wo_block[32 * j:32 * j + DH, j, :], wo).then_inc(wo_loaded, 16)
                sp.dma_start(wo_block[32 * j + DH:32 * j + DH + 1, j, :], bo.rearrange("(a d) -> a d", a=1)).then_inc(wo_loaded, 16)
            load_max(0, 0)

            def sequence(b, last):
                for q in range(QUADS):
                    if not last or q < QUADS - 1:
                        load_max(b * QUADS + q + 1, (q + 1) % QUADS)
                    if not last:
                        sp.wait_ge(b_ready, b_place(b, q, steps_n - 1)[1] + 1)
                        rows.load(sp, b + 1, q, range(rows.load_dmas))

            with sp.Fori(0, B - 1) as b:
                sequence(b, False)
            sequence(B - 1, True)

        @block.gpsimd
        def _(pool):
            steps = Steps(pool, pool_steps_sem)
            pool.sem_inc(z_turned, 1)
            pool.sem_inc(values_taken, 1)
            pool.memset(wo_block[:, :, :], 0.0).then_inc(wo_zeroed, 1)
            pool.wait_ge(wo_zeroed, 1)
            for q in range(QUADS):
                ins = pool.memset(k_rows[q][SROWS:SROWS + MROWS, :, :], 1.0)
            ins.then_inc(ones_ready, 1)
            pool.wait_ge(ones_ready, 1)

            def copy(b, q):
                pool.tensor_copy(v_now[:, q, :, :],
                                 v_res[:, bass.ds(b * QT, QT), q * QUAD:(q + 1) * QUAD, :]
                                 .rearrange("p t h d -> p t (h d)")).then_inc(v_copied, 1)

            def head_sum(b, q):
                pool.wait_ge(inv_ready, b * QUADS + q + 1)
                ins = pool.tensor_tensor(weighted[:, :, :, :], values[:, :, :, 0:DH],
                                         inv[:, :, :, :].broadcast_to([P, QT, QUAD, DH]), ALU.mult)
                ins.then_inc(values_taken, 1)
                pool.wait_ge(values_taken, b * QUADS + q + 2)
                steps.then(pool.tensor_tensor(pairs[:, :, :, :], weighted[:, :, 0:2, :], weighted[:, :, 2:4, :], ALU.add))
                if q == 0:
                    pool.wait_ge(z_turned, b + 1)
                    steps.then(pool.tensor_tensor(z[:, :, 0:DH], pairs[:, :, 0, :], pairs[:, :, 1, :], ALU.add))
                    return
                steps.then(pool.tensor_tensor(z[:, :, 0:DH], z[:, :, 0:DH], pairs[:, :, 0, :], ALU.add))
                ins = pool.tensor_tensor(z[:, :, 0:DH], z[:, :, 0:DH], pairs[:, :, 1, :], ALU.add)
                if q < QUADS - 1:
                    steps.then(ins)
                else:
                    ins.then_inc(z_ready, 1)

            def clear_masked(b, q, kt, first=False):
                b, q = b + q // QUADS, q % QUADS
                pool.wait_ge(b_free, b_place(b, q, last_slot[kt], first)[1] + 3)
                pool.sem_inc(mask_begun, 1)
                blocks = prob[PROB[kt]][:, :, prob_at(kt, kt * P):prob_at(kt, kt * P) + P]
                pool.affine_select(out=blocks, in_=blocks, compare_op=ALU.is_ge, fill=0.0, base=0,
                                   pattern=[[0, QUAD], [1, P]], channel_multiplier=-1).then_inc(masked, 1)

            for q in range(QUADS):
                copy(0, q)
            steps.then(pool.memset(z[:, :, :], 0.0))
            steps.then(pool.memset(z[:, :, DH:DH + 1], float(H)))

            def sequence(b, last):
                for q in range(QUADS):
                    more = not last or q < QUADS - 1
                    for kt in range(lead_kts, QT):
                        clear_masked(b, q, kt)
                    if more:
                        clear_masked(b, q + 1, 0)
                    if not last:
                        pool.wait_ge(pv_ready, (b * QUADS + q + 1) * QT + QT)
                        copy(b + 1, q)
                    head_sum(b, q)
                    if more:
                        for kt in range(1, lead_kts):
                            clear_masked(b, q + 1, kt)

            for kt in range(lead_kts):
                clear_masked(0, 0, kt, True)

            at = steps.n
            per = 2 + 3 * (QUADS - 2) + 2
            with pool.Fori(0, B - 1) as b:
                steps.base = b * per
                sequence(b, False)
                assert steps.n - at == per, (steps.n - at, per)
            steps.base = (B - 2) * per
            sequence(B - 1, True)

        @block.scalar
        def _(act):
            act.sem_inc(b_free, 2)
            act.sem_inc(o_copied, 1)
            act.wait_ge(wo_zeroed, 1)
            act.activation(o_ps[:, :], wo_block[:, :, :].rearrange("p j d -> p (j d)"), ACT.Copy).then_inc(o_zeroed, 1)

            def exponentials(b, q, n, first=False):
                kt, h, heads = slots[n]
                b, q = b + q // QUADS, q % QUADS
                slot, number = b_place(b, q, n, first)
                act.wait_ge(b_ready, number + 1)
                if h == 0:
                    before = max((k for k in range(kt) if PROB[k] == PROB[kt]), default=None)
                    if before is None:
                        before = max(k for k in range(QT) if PROB[k] == PROB[kt]) - QT
                    act.wait_ge(pv_ready, (b * QUADS + q) * QT + before + 1 + QT)
                at = kt * P if heads == 1 else 0
                act.activation(prob[PROB[kt]][:, h:h + heads, prob_at(kt, kt * P):prob_at(kt, S)],
                               b_ps[:, slot, :].rearrange("p (h t) -> p h t", h=heads)[:, :, at:at + S - kt * P],
                               ACT.Exp, scale=float(DH) ** -0.5).then_inc(b_free, 1)

            def finish(b, q, n, more):
                u = b * QUADS + q
                if n == COPY_AT:
                    act.wait_ge(pv_ready, (u + 1) * QT + QT)
                    act.activation(o_sb[:, :], o_ps[:, :], ACT.Copy).then_inc(o_copied, 1)
                if n == TURN_AT:
                    slot, number = b_place_values(b, q, more)
                    act.wait_ge(b_ready, number + 1)
                    act.wait_ge(values_taken, u + 1)
                    act.activation(values[:, :, :, :],
                                   b_ps[:, slot, :].rearrange("p (t h r) -> p t h r", t=QT, h=QUAD)[:, :, :, 0:DH + 1],
                                   ACT.Copy).then_inc(b_free, 1)

            def sequence(b, last):
                for q in range(QUADS):
                    more = not last or q < QUADS - 1
                    for n in range(LEAD, steps_n):
                        exponentials(b, q, n)
                    for n in range(LEAD):
                        if more:
                            exponentials(b, q + 1, n)
                        finish(b, q, n, more)

            for n in range(LEAD):
                exponentials(0, 0, n, True)
            with act.Fori(0, B - 1) as b:
                sequence(b, False)
            sequence(B - 1, True)

        @block.vector
        def _(dve):
            steps = Steps(dve, steps_sem)
            ring = Ring()
            dve.sem_inc(a_free, 2)

            def query_maxima(item, q):
                qt, first, keys, _, h, heads = item
                bank, number = ring.take()
                dve.wait_ge(a_ready, number + 1)
                dst = max_b[:, q % 2, h:h + heads, qt - QT // 2] if first else max_a[:, q % 2, h:h + heads, qt]
                dve.tensor_reduce(dst, a_ps[:, bank, 0:heads * keys].rearrange("p (h k) -> p h k", h=heads),
                                  AX.X, ALU.max).then_inc(a_free, 1)

            def join_maxima(q):
                dve.wait_ge(a_free, ring.base + ring.n + 2)
                dve.tensor_tensor(max_a[:, q % 2, :, QT // 2:], max_a[:, q % 2, :, QT // 2:], max_b[:, q % 2, :, :],
                                  ALU.max).then_inc(max_ready, 1)

            def cut_maxima():
                bank, number = ring.take()
                dve.wait_ge(a_ready, number + 1)
                ins = dve.tensor_scalar(neg_max[:, :], a_ps[0:QUAD * QT, bank, 0:P], -1.0, None, ALU.mult)
                ins.then_inc(a_free, 1)
                dve.wait_ge(a_free, number + 3)
                steps.then(dve.tensor_copy(max_parts[:, 0, :], neg_max[:, :]))
                dve.tensor_tensor(max_parts[:, 1, :], neg_max[:, :], max_parts[:, 0, :], ALU.subtract).then_inc(max_cut, 1)

            def invert(b, q, more):
                dve.wait_ge(b_free, b_place_values(b, q, more)[1] + 3)
                dve.wait_ge(values_taken, b * QUADS + q + 1)
                dve.reciprocal(inv[:, :, :, :], values[:, :, :, DH:DH + 1]).then_inc(inv_ready, 1)

            def take_z():
                for i in range(2):
                    bank, number = ring.take()
                    dve.wait_ge(a_ready, number + 1)
                    ins = dve.tensor_copy(z_t[:, i, :], a_ps[:, bank, 0:P])
                    ins.then_inc(a_free, 1)
                dve.wait_ge(a_free, number + 3)
                dve.sem_inc(z_turned, 1)

            def add_output(b):
                for i in range(QT // 2):
                    bank, number = ring.take()
                    dve.wait_ge(a_ready, number + 1)
                    xs = x_res[:, bass.ds(b * QT + 2 * i, 2), :]
                    dve.tensor_tensor(xs, xs, a_ps[:, bank, :].rearrange("p (j d) -> p j d", j=2),
                                      ALU.add).then_inc(a_free, 1)

            for item in banks:
                query_maxima(item, 0)
            join_maxima(0)
            for i, item in enumerate(banks[:early]):
                query_maxima(item, 1)
                if i == 1:
                    cut_maxima()

            def step(q, n, more, more2):
                items, ahead = beside(n)
                if more if ahead == 1 else more2:
                    for item in items:
                        query_maxima(item, q + ahead)
                if more and n == AHEAD - 1:
                    join_maxima(q + 1)
                if more and n == AHEAD + 1:
                    cut_maxima()

            for n in range(LEAD):
                step(0, n, True, True)

            def sequence(b, last):
                ring.sequence(b)
                for q in range(QUADS):
                    more = not last or q < QUADS - 1
                    more2 = not last or q < QUADS - 2
                    for n in range(LEAD, steps_n):
                        step(q, n, more, more2)
                    for n in range(LEAD):
                        if more:
                            step(q + 1, n, more2, None)
                        if n == INVERT_AT:
                            invert(b, q, more)
                        if q == QUADS - 1 and n == OUTPUT_AT:
                            take_z()
                        if q == QUADS - 1 and n == OUTPUT_AT + 1:
                            add_output(b)

            at = steps.n
            per = QUADS
            with dve.Fori(0, B - 1) as b:
                steps.base = b * per
                sequence(b, False)
                assert steps.n - at == per, (steps.n - at, per)
            steps.base = (B - 2) * per
            sequence(B - 1, True)

        @block.tensor
        def _(pe):
            ring = Ring()
            pe.sem_inc(pv_ready, QT)

            def query_major(item, q):
                qt, first, keys, diagonal, h0, heads = item
                q %= QUADS
                bank, number = ring.take()
                pe.wait_ge(a_free, number + 1)
                for i in range(heads):
                    end = (i + 1) * keys
                    ins = pe.matmul(a_ps[:, bank, i * keys:end], q_rows[q][0:SROWS, h0 + i, qt * P:(qt + 1) * P],
                                    k_rows[q][0:SROWS, h0 + i, first:first + keys], start=True, stop=not diagonal)
                    if diagonal:
                        ins = pe.matmul(a_ps[:, bank, end - P:end], ident_b[:, :], mask_qk[:, :],
                                        start=False, stop=True)
                ins.then_inc(a_ready, 1)

            def key_major(b, q, n, part, first=False):
                kt, h0, heads = slots[n]
                slot, number = b_place(b, q, n, first)
                if part == 0:
                    pe.wait_ge(b_free, number + 1)
                depth = SROWS + MROWS
                if heads == 1:
                    at = max(part * HALF, kt * P)
                    products = [(h0, at, (part + 1) * HALF, at)]
                else:
                    products = [(h0 + i, kt * P, S, i * S // heads) for i in range(part * heads // 2, (part + 1) * heads // 2)]
                for h, begin, end, at in products:
                    ins = pe.matmul(b_ps[:, slot, at:at + end - begin], k_rows[q][0:depth, h, kt * P:(kt + 1) * P],
                                    q_rows[q][0:depth, h, begin:end], start=True, stop=True)
                if part == 1:
                    ins.then_inc(b_ready, 1)

            def weigh(b, q, n, first=False):
                u = b * QUADS + q
                for kt, places in enumerate(WEIGH):
                    if n not in places:
                        continue
                    quarter = quarters(kt)[places.index(n)]
                    at, end = max(quarter * QUARTER, kt * P), (quarter + 1) * QUARTER
                    if n == places[0]:
                        pe.wait_ge(b_free, b_place(b, q, last_slot[kt], first)[1] + 3)
                        if kt == 0:
                            pe.wait_ge(v_copied, u + 1)
                            pe.wait_ge(o_copied, u + 1)
                    if n == places[-1]:
                        pe.wait_ge(masked, u * QT + kt + 1)
                    for h in range(QUAD):
                        ins = pe.matmul(o_ps[32 * h:32 * h + DH + 1, at:end],
                                        v_now[:, q, kt, h * (DH + 1):(h + 1) * (DH + 1)],
                                        prob[PROB[kt]][:, h, prob_at(kt, at):prob_at(kt, end)],
                                        start=(kt == 0 and quarter in (1, 2)),
                                        stop=(kt == (at // HALF + 1) * HALF // P - 1))
                    if n == places[-1]:
                        ins.then_inc(pv_ready, 1)

            def turn_maxima(u, q):
                bank, number = ring.take()
                pe.wait_ge(a_free, number + 1)
                pe.wait_ge(max_ready, u + 1)
                pe.transpose(a_ps[0:QUAD * QT, bank, 0:P], max_a[:, q % 2, :, :].rearrange("p h t -> p (h t)"),
                             ident[:, :]).then_inc(a_ready, 1)

            def turn_values(b, q, more):
                slot, number = b_place_values(b, q, more)
                pe.wait_ge(b_free, number + 1)
                pe.wait_ge(o_copied, b * QUADS + q + 2)
                for qt in range(QT):
                    ins = pe.transpose(b_ps[:, slot, qt * P:(qt + 1) * P], o_sb[:, qt * P:(qt + 1) * P], ident[:, :])
                ins.then_inc(b_ready, 1)

            def turn_z(b):
                for i in range(2):
                    bank, number = ring.take()
                    pe.wait_ge(a_free, number + 1)
                    pe.wait_ge(z_ready, b + 1)
                    pe.transpose(a_ps[:, bank, 0:P],
                                 z[:, i * QT // 2:(i + 1) * QT // 2, :].rearrange("p t d -> p (t d)"),
                                 ident[:, :]).then_inc(a_ready, 1)

            def output(b):
                pe.wait_ge(z_turned, b + 2)
                for i in range(QT // 2):
                    bank, number = ring.take()
                    pe.wait_ge(a_free, number + 1)
                    pe.matmul(a_ps[:, bank, :], z_t[:, i // 2, :],
                              wo_block[:, 2 * (i % 2):2 * (i % 2) + 2, :].rearrange("p j d -> p (j d)"),
                              start=True, stop=True).then_inc(a_ready, 1)

            def step(b, q, n, more, more2, first=False):
                u = b * QUADS + q
                if n == 0:
                    pe.wait_ge(max_loaded, 16 * MROWS * (u + 1))
                items, ahead = beside(n)
                if not (more if ahead == 1 else more2):
                    items = []
                elif n == AHEAD:
                    pe.wait_ge(qk_loaded[(q + 2) % QUADS], rows.load_incs * (b + 1 + (q + 2) // QUADS))
                for item in items[:1]:
                    query_major(item, q + ahead)
                key_major(b, q, n, 0, first)
                key_major(b, q, n, 1, first)
                for item in items[1:]:
                    query_major(item, q + ahead)
                if more and n == AHEAD + 1:
                    turn_maxima(u + 1, q + 1)
                weigh(b, q, n, first)

            pe.wait_ge(qk_loaded[0], rows.load_incs)
            for item in banks:
                query_major(item, 0)
            pe.wait_ge(qk_loaded[1], rows.load_incs)
            for i, item in enumerate(banks[:early]):
                query_major(item, 1)
                if i == 1:
                    turn_maxima(0, 0)
            pe.wait_ge(ones_ready, 1)
            pe.wait_ge(o_zeroed, 1)
            for n in range(LEAD):
                step(0, 0, n, True, True, True)
            pe.wait_ge(wo_loaded, 16 * QT)

            def sequence(b, last):
                ring.sequence(b)
                for q in range(QUADS):
                    more = not last or q < QUADS - 1
                    more2 = not last or q < QUADS - 2
                    for n in range(LEAD, steps_n):
                        step(b, q, n, more, more2)
                    for n in range(LEAD):
                        if more:
                            step(b + (q + 1) // QUADS, (q + 1) % QUADS, n, more2, None)
                        weigh(b, q, steps_n + n)
                        if n == TURN_AT:
                            turn_values(b, q, more)
                        if q == QUADS - 1 and n == OUTPUT_AT:
                            turn_z(b)
                        if q == QUADS - 1 and n == OUTPUT_AT + 1:
                            output(b)

            with pe.Fori(0, B - 1) as b:
                sequence(b, False)
            sequence(B - 1, True)


def constants(nc, ident, ident_b, mask_qk):
    with ExitStack() as ctx:
        filled = ctx.enter_context(nc.semaphore("filled"))
        made = ctx.enter_context(nc.semaphore("made"))
        block = ctx.enter_context(nc.Block())

        @block.gpsimd
        def _(pool):
            for t in (ident, ident_b, mask_qk):
                ins = pool.memset(t[:, :], 0.0)
                ins.then_inc(filled, 1)
            pool.wait_ge(filled, 3)
            for t in (ident, ident_b):
                pool.affine_select(out=t[:, :], in_=t[:, :], compare_op=ALU.not_equal, fill=1.0, base=0,
                                   pattern=[[-1, P]], channel_multiplier=1).then_inc(made, 1)
            pool.affine_select(out=mask_qk[:, :], in_=mask_qk[:, :], compare_op=ALU.is_ge, fill=NEG, base=0,
                               pattern=[[-1, P]], channel_multiplier=1).then_inc(made, 1)
            pool.wait_ge(made, 3)


def program(nc, x, wq, bq, wk, bk, wv, bv, wo, bo, gate_w, w1, w3, w2, out):
    with ExitStack() as ctx:
        def sb(n, shape, dt):
            return ctx.enter_context(nc.sbuf_tensor(n, shape, dt))

        x_res = sb("x_res", [P, TILES, D], F32)
        ident = sb("ident", [P, P], F32)
        ident_b = sb("ident_b", [P, P], BF16)
        mask_qk = sb("mask_qk", [P, P], BF16)
        constants(nc, ident, ident_b, mask_qk)
        parts = nc.dram_tensor("qk_parts", [2, 3, D, TOKENS], BF16, kind="Internal").ap()
        with ExitStack() as norm_ctx, ExitStack() as attn_ctx:
            norm = Norm(nc, norm_ctx, "norm1")
            ffn(nc, "ffn1", norm, x, x_res, ident, gate_w, w1, w3, w2, None)
            v_res = attn_ctx.enter_context(nc.sbuf_tensor("v_res", [P, TILES, H, DH + 1], F32))
            rows = Rows(nc, attn_ctx, parts)
            project(nc, norm, x_res, v_res, ident, (wq, wk, wv), (bq, bk, bv), parts, rows)
            norm_ctx.close()
            attention(nc, x_res, v_res, ident, ident_b, mask_qk, wo, bo, rows)
        with ExitStack() as norm_ctx:
            ffn(nc, "ffn2", Norm(nc, norm_ctx, "norm2"), None, x_res, ident, gate_w, w1, w3, w2, out)


_INS = ["L0_attn_x", "L0_attn_WQ", "L0_attn_bQ", "L0_attn_WK", "L0_attn_bK", "L0_attn_WV", "L0_attn_bV",
        "L0_attn_WO", "L0_attn_bO", "L0_ffn_gate_w", "L0_ffn_w1", "L0_ffn_w3", "L0_ffn_w2"]


def kernel(**inputs):
    import numpy as _np
    import concourse.bacc as _bacc
    from concourse import mybir as _mybir
    from concourse.bass_utils import run_bass_kernel_spmd as _run

    nc = _bacc.Bacc("TRN2", target_bir_lowering=False, num_devices=1)
    arrays, args = {}, []
    for name in _INS:
        a = _np.ascontiguousarray(inputs[name])
        arrays[f"in_{name}_dram"] = a
        args.append(nc.dram_tensor(f"in_{name}_dram", a.shape, _mybir.dt.from_np(a.dtype), kind="ExternalInput").ap())
    args.append(nc.dram_tensor("out_0_dram", (B, S, D), F32, kind="ExternalOutput").ap())
    program(nc, *args)
    r = _run(nc, [arrays], core_ids=[0])
    return r.results[0]["out_0_dram"]
```
